# Optimizing a Trainium2 kernel written in Bass

```python
import numpy as np
import jax
import jax.numpy as jnp

def _softmax(x, axis=-1):
    return jax.nn.softmax(x, axis=axis)

def _gelu(x):
    return jax.nn.gelu(x, approximate=True)

def _silu(x):
    return jax.nn.silu(x)

def _sigmoid(x):
    return jax.nn.sigmoid(x)

def _layernorm(x, axis=-1, eps=1e-05):
    m = jnp.mean(x, axis=axis, keepdims=True)
    v = jnp.var(x, axis=axis, keepdims=True)
    return (x - m) / jnp.sqrt(v + eps)

def _scatter_add(tgt, idx, src, axis=0):
    return tgt.at[idx].add(src)

def _segment_sum(src, seg, n):
    return jax.ops.segment_sum(src, seg, n)
kernel_name = 'mk_cond_resid_d4_seqx_r4_cc8392'

def setup_inputs(seed: int=0):
    np.random.seed(seed)
    _w = jnp.asarray

    def _rec_inputs():
        import jax
        import jax.numpy as jnp
        _rk = jax.random.key(seed)
        x = -0.0002071 + 1 * jax.random.normal(jax.random.fold_in(_rk, 1), (2, 1024, 256), jnp.float32)
        _lenS = 1024 - jax.random.randint(jax.random.fold_in(_rk, 7), (2,), 0, max(1, 1024 // 4) + 1, jnp.int32)
        _lenS2 = 1024 - jax.random.randint(jax.random.fold_in(_rk, 8), (2,), 0, max(1, 1024 // 4) + 1, jnp.int32)
        cond_8 = jax.random.uniform(jax.random.fold_in(_rk, 11), (2, 8), jnp.float32, 0.0, 0.983423)
        return (x, cond_8)
    x, cond_8 = _rec_inputs()

    def _L0_cond_setup():
        import jax, jax.numpy as jnp
        import numpy as np
        R = 16
        ALPHA = 32.0
        SCALING = ALPHA / R
        key = jax.random.key(seed)
        ks = jax.random.split(key, 6)
        B, T, C, O, E = (16, 375, 256, 256, 8)
        x = jax.random.normal(ks[0], (B, T, C), dtype=jnp.float32)
        w = jax.random.uniform(ks[1], (B, E), dtype=jnp.float32)
        W_base = jax.random.normal(ks[2], (O, C), dtype=jnp.float32) * 0.02
        b_base = jax.random.normal(ks[3], (O,), dtype=jnp.float32) * 0.02
        As = jax.random.normal(ks[4], (E, R, C), dtype=jnp.float32) * 0.02
        Bs = jax.random.normal(ks[5], (E, O, R), dtype=jnp.float32) * 0.02
        return {'x': x, 'w': w, 'W_base': W_base, 'b_base': b_base, 'As': As, 'Bs': Bs}
    _L0_cond_all = _L0_cond_setup()
    _L0_cond_in = {k: v for k, v in _L0_cond_all.items() if k in ('W_base', 'b_base', 'As', 'Bs')}
    del _L0_cond_all

    def _L1_cond_setup():
        import jax, jax.numpy as jnp
        import numpy as np
        key = jax.random.key(seed)
        k1, k2, k3, k4, k5 = jax.random.split(key, 5)
        B, N, T, O, G = (32, 64, 256, 256, 8)
        x = jax.random.normal(k1, (B, N, T), dtype=jnp.float32)
        y = jax.random.uniform(k2, (B, G), dtype=jnp.float32)
        weight = jax.random.normal(k3, (G, O, T), dtype=jnp.float32) * (1.0 / np.sqrt(T))
        mask = jax.random.uniform(k4, (O, T), dtype=jnp.float32)
        bias = jax.random.normal(k5, (O,), dtype=jnp.float32)
        return {'x': x, 'y': y, 'weight': weight, 'mask': mask, 'bias': bias}
    _L1_cond_all = _L1_cond_setup()
    _L1_cond_in = {k: v for k, v in _L1_cond_all.items() if k in ('weight', 'mask', 'bias')}
    del _L1_cond_all

    def _L2_cond_setup():
        import jax, jax.numpy as jnp
        import numpy as np
        TOP_K = 2
        NUM_MOE_LAYERS = 12

        def _gemma_mlp(x, gate_w, up_w, down_w):
            g = jnp.einsum('bsh,hi->bsi', x, gate_w)
            u = jnp.einsum('bsh,hi->bsi', x, up_w)
            return jnp.einsum('bsi,ih->bsh', jax.nn.gelu(g, approximate=True) * u, down_w)
        key = jax.random.key(seed)
        ks = jax.random.split(key, 8)
        B, S, H, I, E = (32, 64, 256, 1024, 8)
        std = 0.02
        return {'x': jax.random.normal(ks[0], (B, S, H), jnp.float32), 'router_logits': jax.random.normal(ks[1], (B, E), jnp.float32), 'skill_gate': jax.random.normal(ks[2], (E, H, I), jnp.float32) * std, 'skill_up': jax.random.normal(ks[3], (E, H, I), jnp.float32) * std, 'skill_down': jax.random.normal(ks[4], (E, I, H), jnp.float32) * std, 'shared_gate': jax.random.normal(ks[5], (H, I), jnp.float32) * std, 'shared_up': jax.random.normal(ks[6], (H, I), jnp.float32) * std, 'shared_down': jax.random.normal(ks[7], (I, H), jnp.float32) * std}
    _L2_cond_all = _L2_cond_setup()
    _L2_cond_in = {k: v for k, v in _L2_cond_all.items() if k in ('skill_gate', 'skill_up', 'skill_down', 'shared_gate', 'shared_up', 'shared_down')}
    del _L2_cond_all

    def _L3_cond_setup():
        import jax, jax.numpy as jnp
        import numpy as np
        B, S, D = (16, 512, 256)
        E, H = (8, 512)
        key = jax.random.key(seed)
        ks = jax.random.split(key, 8)
        scale = 0.02
        x = jax.random.normal(ks[0], (B, S, D), dtype=jnp.float32)
        opcode_onehot = jax.random.uniform(ks[1], (B, E), dtype=jnp.float32)
        W_up = jax.random.normal(ks[2], (E, H, D), dtype=jnp.float32) * scale
        b_up = jnp.zeros((E, H), dtype=jnp.float32)
        W_gate = jax.random.normal(ks[3], (E, H, D), dtype=jnp.float32) * scale
        b_gate = jnp.zeros((E, H), dtype=jnp.float32)
        W_down = jax.random.normal(ks[4], (E, D, H), dtype=jnp.float32) * scale
        b_down = jnp.zeros((E, D), dtype=jnp.float32)
        return {'x': x, 'opcode_onehot': opcode_onehot, 'W_up': W_up, 'b_up': b_up, 'W_gate': W_gate, 'b_gate': b_gate, 'W_down': W_down, 'b_down': b_down}
    _L3_cond_all = _L3_cond_setup()
    _L3_cond_in = {k: v for k, v in _L3_cond_all.items() if k in ('W_up', 'b_up', 'W_gate', 'b_gate', 'W_down', 'b_down')}
    del _L3_cond_all
    return {'x': x, 'cond_8': cond_8, 'L0_cond_W_base': _L0_cond_in['W_base'], 'L0_cond_b_base': _L0_cond_in['b_base'], 'L0_cond_As': _L0_cond_in['As'], 'L0_cond_Bs': _L0_cond_in['Bs'], 'L1_cond_weight': _L1_cond_in['weight'], 'L1_cond_mask': _L1_cond_in['mask'], 'L1_cond_bias': _L1_cond_in['bias'], 'L2_cond_skill_gate': _L2_cond_in['skill_gate'], 'L2_cond_skill_up': _L2_cond_in['skill_up'], 'L2_cond_skill_down': _L2_cond_in['skill_down'], 'L2_cond_shared_gate': _L2_cond_in['shared_gate'], 'L2_cond_shared_up': _L2_cond_in['shared_up'], 'L2_cond_shared_down': _L2_cond_in['shared_down'], 'L3_cond_W_up': _L3_cond_in['W_up'], 'L3_cond_b_up': _L3_cond_in['b_up'], 'L3_cond_W_gate': _L3_cond_in['W_gate'], 'L3_cond_b_gate': _L3_cond_in['b_gate'], 'L3_cond_W_down': _L3_cond_in['W_down'], 'L3_cond_b_down': _L3_cond_in['b_down']}

def reference(x, cond_8, L0_cond_W_base, L0_cond_b_base, L0_cond_As, L0_cond_Bs, L1_cond_weight, L1_cond_mask, L1_cond_bias, L2_cond_skill_gate, L2_cond_skill_up, L2_cond_skill_down, L2_cond_shared_gate, L2_cond_shared_up, L2_cond_shared_down, L3_cond_W_up, L3_cond_b_up, L3_cond_W_gate, L3_cond_b_gate, L3_cond_W_down, L3_cond_b_down):
    import jax
    import jax.numpy as jnp

    def _L0_cond_ref(x, w, W_base, b_base, As, Bs):
        import jax, jax.numpy as jnp
        import numpy as np
        R = 16
        ALPHA = 32.0
        SCALING = ALPHA / R
        out = jnp.einsum('btc,oc->bto', x, W_base) + b_base
        h = jnp.einsum('btc,erc->bter', x, As)
        lora = jnp.einsum('bter,eor,be->bto', h, Bs, w)
        return out + lora * SCALING

    def _L1_cond_ref(x, y, weight, mask, bias):
        import jax, jax.numpy as jnp
        import numpy as np
        masked_w = weight * mask[None, :, :]
        w_bot = jnp.einsum('bg,got->bot', y, masked_w)
        return jnp.einsum('bnt,bot->bno', x, w_bot) + bias

    def _L2_cond_ref(x, router_logits, skill_gate, skill_up, skill_down, shared_gate, shared_up, shared_down):
        import jax, jax.numpy as jnp
        import numpy as np
        TOP_K = 2
        NUM_MOE_LAYERS = 12

        def _gemma_mlp(x, gate_w, up_w, down_w):
            g = jnp.einsum('bsh,hi->bsi', x, gate_w)
            u = jnp.einsum('bsh,hi->bsi', x, up_w)
            return jnp.einsum('bsi,ih->bsh', jax.nn.gelu(g, approximate=True) * u, down_w)
        B = x.shape[0]
        E = skill_gate.shape[0]
        rw = jax.nn.softmax(router_logits.astype(jnp.float32), axis=-1)
        w, sel = jax.lax.top_k(rw, TOP_K)
        w = w / w.sum(axis=-1, keepdims=True)
        w = w.astype(x.dtype)
        scale = 1.0 / NUM_MOE_LAYERS
        w = scale * w + (1.0 - scale) * jax.lax.stop_gradient(w)
        dense_w = jnp.zeros((B, E), x.dtype).at[jnp.arange(B)[:, None], sel].add(w)

        def step(acc, params):
            g, u, d, we = params
            return (acc + we[:, None, None] * _gemma_mlp(x, g, u, d), None)
        out, _ = jax.lax.scan(step, jnp.zeros_like(x), (skill_gate, skill_up, skill_down, dense_w.T))
        out = out + _gemma_mlp(x, shared_gate, shared_up, shared_down)
        return out

    def _L3_cond_ref(x, opcode_onehot, W_up, b_up, W_gate, b_gate, W_down, b_down):
        import jax, jax.numpy as jnp
        import numpy as np
        B, S, D = (16, 512, 256)
        E, H = (8, 512)
        expert = jnp.argmax(opcode_onehot, axis=-1)
        wu, bu = (W_up[expert], b_up[expert])
        wg, bg = (W_gate[expert], b_gate[expert])
        wd, bd = (W_down[expert], b_down[expert])
        up = jnp.einsum('bsd,bhd->bsh', x, wu) + bu[:, None, :]
        gate = jnp.einsum('bsd,bhd->bsh', x, wg) + bg[:, None, :]
        hidden = jax.nn.silu(up) * gate
        out = jnp.einsum('bsh,bdh->bsd', hidden, wd) + bd[:, None, :]
        return out
    x = x + _L0_cond_ref(x, cond_8, L0_cond_W_base, L0_cond_b_base, L0_cond_As, L0_cond_Bs)
    x = x + _L1_cond_ref(x, cond_8, L1_cond_weight, L1_cond_mask, L1_cond_bias)
    x = x + _L2_cond_ref(x, cond_8, L2_cond_skill_gate, L2_cond_skill_up, L2_cond_skill_down, L2_cond_shared_gate, L2_cond_shared_up, L2_cond_shared_down)
    x = x + _L3_cond_ref(x, cond_8, L3_cond_W_up, L3_cond_b_up, L3_cond_W_gate, L3_cond_b_gate, L3_cond_W_down, L3_cond_b_down)
    return x

_drawn_inputs = setup_inputs


def setup_inputs(seed=0):
    import zlib

    import numpy as np

    out = dict(_drawn_inputs(seed))
    spreads = {'L3_cond_b_up': (0.0, 0.8), 'L3_cond_b_gate': (0.0, 0.8), 'L3_cond_b_down': (0.0, 0.1)}
    factors = {'L0_cond_b_base': 4.13}
    for name, (base, spread) in spreads.items():
        noise = np.random.default_rng([zlib.crc32(name.encode()), seed]).standard_normal(out[name].shape)
        drawn = base * np.exp(spread * noise) if base else spread * noise
        out[name] = jnp.asarray(drawn.astype(out[name].dtype))
    for name, factor in factors.items():
        out[name] = (out[name] * factor).astype(out[name].dtype)
    return out
```

```python
from contextlib import ExitStack

import concourse.bass as bass
from concourse import mybir

F32 = mybir.dt.float32
F32R = mybir.dt.float32r
U32 = mybir.dt.uint32
ALU = mybir.AluOpType
ACT = mybir.ActivationFunctionType

P = 128
MOVE = 512
LORA_SCALING = 32.0 / 16.0
MOE_SCALE = 1.0 / 12.0


def cond_residual_stack(nc, x, cond, w_base, b_base, lora_a, lora_b, l1_w, l1_mask, l1_bias,
                        moe_gate, moe_up, moe_down, sh_gate, sh_up, sh_down,
                        w_up, b_up, w_gate, b_gate, w_down, b_down, out):
    B, T, D = x.shape
    G = cond.shape[1]
    R = lora_a.shape[1]
    KD = D // P
    TB = T // P
    CH = T // MOVE
    TC = MOVE // P
    UPQ = 4
    QW = UPQ * P
    QPP = moe_gate.shape[2] // QW
    UPP = QPP * UPQ
    PASSES = 3
    L3U = w_up.shape[1] // P
    G2U = PASSES * UPP
    UNIT0 = [0, G2U, 2 * G2U, 2 * G2U + L3U, 2 * G2U + 2 * L3U]
    END = [CH * u for u in UNIT0[1:]]
    assert (KD, CH, B, L3U, QPP, G * R) == (2, 2, 2, UPQ, 2, P)
    SLOT = 3 * 16

    x_t = x.rearrange("b (t p) d -> p b t d", p=P)
    out_t = out.rearrange("b (t p) d -> p b t d", p=P)

    with ExitStack() as ctx:
        def sb(name, shape, dt=F32):
            return ctx.enter_context(nc.sbuf_tensor(name, shape, dt))

        def sem(name):
            return ctx.enter_context(nc.semaphore(name))

        x_f = sb("x_f", [P, KD, B * T])
        x_hi = sb("x_hi", [P, KD, B * T], F32R)
        x_lo = sb("x_lo", [P, KD, B * T], F32R)
        x_nat = sb("x_nat", [P, B, TB, D])
        g_f = sb("g_f", [P, 2, MOVE])
        h_f = sb("h_f", [P, 2, MOVE])
        h_hi = sb("h_hi", [P, 2, MOVE], F32R)
        h_lo = sb("h_lo", [P, 2, MOVE], F32R)
        raw_gu = sb("raw_gu", [P, QPP, 2, KD, QW])
        raw_dn = sb("raw_dn", [P, QPP, UPQ, D])
        gu_hi = sb("gu_hi", [P, 2, 2 * KD, P], F32R)
        gu_lo = sb("gu_lo", [P, 2, 2 * KD, P], F32R)
        dn_hi = sb("dn_hi", [P, 2, D], F32R)
        dn_lo = sb("dn_lo", [P, 2, D], F32R)
        l3_w = sb("l3_w", [P, B, L3U, 2 * KD * P + D])
        l1_nat = sb("l1_nat", [P, G, KD, D])
        diag = sb("diag", [P, G, B, P])
        l3_ug = l1_nat[:, :, :, :].rearrange("p (b a h) k d -> p b a (h k) d", b=B, a=2)
        l3_dn = diag[:, :, :, :].rearrange("p (b m h) c q -> p b m (h c q)", b=B, m=KD)
        ident = sb("ident", [P, P])
        bs_nat = sb("bs_nat", [P, KD, G, R])
        bs_t = sb("bs_t", [P, D])
        as_nat = sb("as_nat", [P, D])
        as_w = sb("as_w", [P, B, D])
        wb = sb("wb", [P, KD, D])
        mask_nat = sb("mask_nat", [P, KD, D])
        mask_t = sb("mask_t", [P, KD, D])
        w0i = sb("w0i", [P, KD, B, D])
        w1it = sb("w1it", [P, KD, B, D])
        m_hi = sb("m_hi", [P, B, KD, D], F32R)
        m_lo = sb("m_lo", [P, B, KD, D], F32R)
        b0_col = sb("b0_col", [P, KD])
        b1_col = sb("b1_col", [P, KD])
        b_eff = sb("b_eff", [P, B, KD])
        cond_r = sb("cond_r", [P, B, G])
        cond_er = sb("cond_er", [P, B])
        top_v = sb("top_v", [P, B, 8])
        top_i = sb("top_i", [P, B, 8], U32)
        neg_m = sb("neg_m", [P, B])
        top_e = sb("top_e", [P, B, 8])
        r_sum = sb("r_sum", [P, B])
        r_inv = sb("r_inv", [P, B])
        top_p = sb("top_p", [P, B, 2])
        w_raw = sb("w_raw", [P, B, 2])
        w_part = sb("w_part", [P, B, 2])
        w_pass = sb("w_pass", [P, B, PASSES])
        bu_col = sb("bu_col", [P, B, L3U])
        bg_col = sb("bg_col", [P, B, L3U])
        bd_col = sb("bd_col", [P, B, KD])

        banks = [ctx.enter_context(nc.psum_tensor(f"bank{n}", [P, MOVE], F32)) for n in range(8)]
        acc = banks[0:4]
        act_ps, lin_ps = banks[4], banks[5]
        tp_ps = banks[6:8]

        s_cond, s_er, s_bs, s_as, s_wb, s_mask, s_b0, s_b1 = (
            sem(n) for n in ("cond_in", "er_in", "bs_in", "as_in", "wb_in", "mask_in", "b0_in", "b1_in"))
        s_x = [sem(f"x_in{b}") for b in range(B)]
        s_l1 = [sem(f"l1_in{n}") for n in range(G // 2)]
        s_raw = [sem(f"raw_in{n}") for n in range(QPP)]
        s_l3 = [sem(f"l3_in{b}") for b in range(B)]
        s_bias = [sem(f"l3_bias_in{b}") for b in range(B)]
        zeroed, ident_ok, diag_ok, wbi_ok, asw_ok = (
            sem(n) for n in ("zeroed", "ident_ok", "diag_ok", "wbi_ok", "asw_ok"))
        bst_tp, bst_ok, maskt_tp, maskt_ok = (sem(n) for n in ("bst_tp", "bst_ok", "maskt_tp", "maskt_ok"))
        xt_tp, xt_hi, xt_lo = (sem(n) for n in ("xt_tp", "xt_hi", "xt_lo"))
        w0_mm, w0_ok, w1_mm, w1_masked, w1_ok = (
            sem(n) for n in ("w0_mm", "w0_ok", "w1_mm", "w1_masked", "w1_ok"))
        m_mm, mhi_ok, mlo_ok, be_mm, be_ok = (sem(n) for n in ("m_mm", "mhi_ok", "mlo_ok", "be_mm", "be_ok"))
        x2_mm, x2_f, x2_hi, x2_lo = (sem(n) for n in ("x2_mm", "x2_f", "x2_hi", "x2_lo"))
        r_max, r_idx, r_neg, r_exp, r_inv_ok, r_p, r_s2, r_w = (
            sem(n) for n in ("r_max", "r_idx", "r_neg", "r_exp", "r_inv_ok", "r_p", "r_s2", "r_w"))
        guhi_ok, gulo_ok, dnhi_ok, dnlo_ok = (sem(n) for n in ("guhi_ok", "gulo_ok", "dnhi_ok", "dnlo_ok"))
        act_mm, lin_mm, g_ok, h_ok, hhi_ok, hlo_ok, down_mm = (
            sem(n) for n in ("act_mm", "lin_mm", "g_ok", "h_ok", "hhi_ok", "hlo_ok", "down_mm"))
        acc_out = sem("acc_out")
        x3_hi, x3_lo = sem("x3_hi"), sem("x3_lo")
        l3_tp, l3_ok = sem("l3_tp"), sem("l3_ok")
        out_tp = [sem(f"out_tp{n}") for n in range(2)]
        out_ok = [sem(f"out_ok{n}") for n in range(2)]
        stored = sem("stored")

        block = ctx.enter_context(nc.Block())

        def tokens(b, c):
            return slice(b * T + c * MOVE, b * T + (c + 1) * MOVE)

        def x2_bank(b, c, m):
            return banks[4 + 2 * c + m] if b == 0 else banks[2 * c + m]

        def l2_unit(j):
            return j // UPQ, j % UPQ

        @block.sync
        def _(sp):
            for n in range(G // 2):
                sp.dma_start(l1_nat[:, 2 * n:2 * n + 2, :, :].rearrange("p g k d -> p (g k) d"),
                             l1_w[2 * n:2 * n + 2, :, :].rearrange("g (k p) d -> p (g k) d", p=P)
                             ).then_inc(s_l1[n], 16)

            def load_quad(slot, gate, up, down):
                cols = slice(slot * QW, (slot + 1) * QW)
                for a, w in ((0, gate), (1, up)):
                    sp.dma_start(raw_gu[:, slot, a, :, :],
                                 w[:, cols].rearrange("(k p) c -> p k c", p=P)).then_inc(s_raw[slot], 16)
                sp.dma_start(raw_dn[:, slot, :, :],
                             down[cols, :].rearrange("(j p) d -> p j d", p=P)).then_inc(s_raw[slot], 16)

            for slot in range(QPP):
                load_quad(slot, sh_gate, sh_up, sh_down)
            sp.dma_start(x_nat[:, 1, :, :], x_t[:, 1, :, :]).then_inc(s_x[1], 16)

            def load_l3(b):
                e = sp.value_load(top_i[0:1, b, 0:1], min_val=0, max_val=G - 1)
                for a, w in ((0, w_up), (1, w_gate)):
                    sp.dma_start(l3_ug[:, b, a, :, :],
                                 w[bass.ds(e, 1), :, :].rearrange("o (j p) d -> p (o j) d", p=P)
                                 ).then_inc(s_l3[b], 16)
                sp.dma_start(l3_dn[:, b, :, :],
                             w_down[bass.ds(e, 1), :, :].rearrange("o (m p) h -> p (o m) h", p=P)
                             ).then_inc(s_l3[b], 16)
                with nc.allow_non_contiguous_dma(reason="bias columns"):
                    for col, v in ((bu_col, b_up), (bg_col, b_gate), (bd_col, b_down)):
                        sp.dma_start(col[:, b, :], v[bass.ds(e, 1), :].rearrange("o (j p) -> p (o j)", p=P)
                                     ).then_inc(s_bias[b], 16)

            sp.wait_ge(r_idx, B)
            sp.wait_ge(w1_mm, KD)
            for b in range(B):
                load_l3(b)

            def freed(q):
                sp.wait_ge(gulo_ok, (q - QPP + 1) * UPQ)
                sp.wait_ge(dnlo_ok, (q - QPP + 1) * UPQ)

            for b in range(B):
                if b:
                    for slot in range(QPP):
                        freed(b * PASSES * QPP + slot)
                        load_quad(slot, sh_gate, sh_up, sh_down)
                with sp.Fori(0, PASSES - 1) as k:
                    e = sp.value_load(top_i[0:1, b, bass.ds(k, 1)], min_val=0, max_val=G - 1)
                    for slot in range(QPP):
                        freed(k * QPP + (b * PASSES + 1) * QPP + slot)
                        cols = slice(slot * QW, (slot + 1) * QW)
                        for a, w in ((0, moe_gate), (1, moe_up)):
                            sp.dma_start(raw_gu[:, slot, a, :, :],
                                         w[bass.ds(e, 1), :, cols].rearrange("o (k p) c -> p (o k) c", p=P)
                                         ).then_inc(s_raw[slot], 16)
                        sp.dma_start(raw_dn[:, slot, :, :],
                                     moe_down[bass.ds(e, 1), cols, :].rearrange("o (j p) d -> p (o j) d", p=P)
                                     ).then_inc(s_raw[slot], 16)

            for b in range(B):
                for c in range(CH):
                    for n in range(2):
                        sp.wait_ge(out_ok[n], b * CH + c + 1)
                        t0 = c * TC + 2 * n
                        sp.dma_start(out_t[:, b, t0:t0 + 2, :], x_nat[:, b, t0:t0 + 2, :]).then_inc(stored, 16)
            sp.wait_ge(stored, 16 * B * CH * 2)

        @block.gpsimd
        def _(pool):
            nc.gpsimd.memset(ident[:, :], 0.0).then_inc(zeroed, 1)
            pool.wait_ge(zeroed, 1)
            nc.gpsimd.affine_select(out=ident[:, :], in_=ident[:, :], compare_op=ALU.not_equal, fill=1.0,
                                    base=0, pattern=[[-1, P]], channel_multiplier=1).then_inc(ident_ok, 1)

            def split_lo(v, slot, gu_src, dn_src):
                pool.wait_ge(guhi_ok, v + 1)
                nc.gpsimd.tensor_tensor(gu_lo[:, slot, :, :], gu_src, gu_hi[:, slot, :, :].bitcast(F32),
                                        ALU.subtract).then_inc(gulo_ok, 1)
                pool.wait_ge(dnhi_ok, v + 1)
                nc.gpsimd.tensor_tensor(dn_lo[:, slot, :], dn_src, dn_hi[:, slot, :].bitcast(F32),
                                        ALU.subtract).then_inc(dnlo_ok, 1)

            def x3_low(b):
                for c in range(CH):
                    for m in range(KD):
                        pool.wait_ge(x3_hi, (b * CH + c) * KD + m + 1)
                        nc.gpsimd.tensor_tensor(x_lo[:, m, tokens(b, c)], x_f[:, m, tokens(b, c)],
                                                x_hi[:, m, tokens(b, c)].bitcast(F32),
                                                ALU.subtract).then_inc(x3_lo, 1)

            def l2_passes(first, last):
                with pool.Fori(first, last) as p:
                    for q in range(QPP):
                        for j in range(UPQ):
                            split_lo(p * UPP + q * UPQ + j, j % 2,
                                     raw_gu[:, q, :, :, j * P:(j + 1) * P].rearrange("p a k c -> p (a k) c"),
                                     raw_dn[:, q, j, :])

            l2_passes(0, PASSES + 1)
            x3_low(0)
            l2_passes(PASSES + 1, 2 * PASSES)
            for b in range(B):
                for j in range(L3U):
                    split_lo(UNIT0[2 + b] + j, j % 2,
                             l3_w[:, b, j, 0:2 * KD * P].rearrange("p (a c) -> p a c", c=P),
                             l3_w[:, b, j, 2 * KD * P:])
                    if b == 0 and j == 2:
                        x3_low(1)

        @block.scalar
        def _(act):
            act.dma_start(cond_r[:, :, :], bass.AP(cond.tensor, 0, [[0, P], [G, B], [1, G]])).then_inc(s_cond, 16)
            act.dma_start(mask_nat[:, :, :], l1_mask.rearrange("(k p) d -> p k d", p=P)).then_inc(s_mask, 16)
            for k in range(KD):
                act.dma_start(bs_nat[:, k, :, :], lora_b[:, k * P:(k + 1) * P, :].rearrange("e p r -> p e r")
                              ).then_inc(s_bs, 16)
            act.dma_start(as_nat[:, :], lora_a.rearrange("e r c -> (e r) c")).then_inc(s_as, 16)
            with nc.allow_non_contiguous_dma(reason="columns"):
                for b in range(B):
                    act.dma_start(cond_er[:, b:b + 1], bass.AP(cond.tensor, b * G, [[1, G], [0, R], [1, 1]])
                                  ).then_inc(s_er, 16)
                act.dma_start(b0_col[:, :], b_base.rearrange("(k p) -> p k", p=P)).then_inc(s_b0, 16)
                act.dma_start(b1_col[:, :], l1_bias.rearrange("(k p) -> p k", p=P)).then_inc(s_b1, 16)
            act.dma_start(wb[:, :, :], w_base.rearrange("(k p) d -> p k d", p=P)).then_inc(s_wb, 16)
            act.dma_start(x_nat[:, 0, :, :], x_t[:, 0, :, :]).then_inc(s_x[0], 16)

            for b in range(B):
                act.wait_ge(r_neg, b + 1)
                nc.scalar.activation(top_e[:, b, :], top_v[:, b, :], ACT.Exp, bias=neg_m[:, b:b + 1],
                                     accum_out=r_sum[:, b:b + 1]).then_inc(r_exp, 1)

            act.wait_ge(bst_tp, 1)
            nc.scalar.activation(bs_t[:, :], tp_ps[0][:, 0:D], ACT.Copy).then_inc(bst_ok, 1)
            act.wait_ge(maskt_tp, 1)
            nc.scalar.activation(mask_t[:, :, :].rearrange("p k d -> p (k d)"), tp_ps[1][:, :], ACT.Copy
                                 ).then_inc(maskt_ok, 1)

            def xt_high(b):
                for n in range(4):
                    act.wait_ge(xt_tp, 4 * b + n + 1)
                    nc.scalar.activation(x_hi[:, n // 2, tokens(b, n % 2)], banks[n][:, :], ACT.Copy
                                         ).then_inc(xt_hi, 1)

            xt_high(0)
            xt_high(1)

            def split_gu(v, slot, src, loaded, count):
                act.wait_ge(loaded, count)
                if not isinstance(v, int) or v >= 2:
                    act.wait_ge(lin_mm, CH * v - CH)
                nc.scalar.activation(gu_hi[:, slot, :, :], src, ACT.Copy).then_inc(guhi_ok, 1)

            def split_dn(v, slot, src, loaded, count):
                act.wait_ge(loaded, count)
                if not isinstance(v, int) or v >= 2:
                    act.wait_ge(down_mm, CH * v - CH)
                nc.scalar.activation(dn_hi[:, slot, :], src, ACT.Copy).then_inc(dnhi_ok, 1)

            def l2_gu(p, j):
                q, u = l2_unit(j)
                split_gu(p * UPP + j, j % 2, raw_gu[:, q, :, :, u * P:(u + 1) * P].rearrange("p a k c -> p (a k) c"),
                         s_raw[q], p * SLOT + SLOT)

            def l2_dn(p, j):
                q, u = l2_unit(j)
                split_dn(p * UPP + j, j % 2, raw_dn[:, q, u, :], s_raw[q], p * SLOT + SLOT)

            def l3_gu(b, j):
                split_gu(UNIT0[2 + b] + j, j % 2,
                         l3_w[:, b, j, 0:2 * KD * P].rearrange("p (a c) -> p a c", c=P),
                         l3_ok, 2 * (b * L3U + j) + 2)

            def l3_dn(b, j):
                split_dn(UNIT0[2 + b] + j, j % 2, l3_w[:, b, j, 2 * KD * P:], l3_ok, 2 * (b * L3U + j) + 2)

            l2_gu(0, 0)
            l2_dn(0, 0)
            l2_gu(0, 1)

            for b in range(B):
                act.wait_ge(m_mm, b + 1)
                nc.scalar.activation(m_hi[:, b, :, :], banks[4 + b][:, :].rearrange("p (k d) -> p k d", k=KD),
                                     ACT.Copy).then_inc(mhi_ok, 1)
            for b in range(B):
                for c in range(CH):
                    for m in range(KD):
                        act.wait_ge(x2_f, (b * CH + c) * KD + m + 1)
                        nc.scalar.activation(x_hi[:, m, tokens(b, c)], x_f[:, m, tokens(b, c)], ACT.Copy
                                             ).then_inc(x2_hi, 1)

            def step(s, c, func, bias):
                act.wait_ge(act_mm, s + 1)
                nc.scalar.activation(g_f[:, c, :], act_ps[:, :], func, bias=bias).then_inc(g_ok, 1)
                act.wait_ge(h_ok, s + 1)
                if not isinstance(s, int) or s >= 2:
                    act.wait_ge(down_mm, s - 1)
                nc.scalar.activation(h_hi[:, c, :], h_f[:, c, :], ACT.Copy).then_inc(hhi_ok, 1)

            def l3_evac(b, j):
                half = 3 * P
                for n in range(2):
                    act.wait_ge(l3_tp, 2 * (b * L3U + j) + n + 1)
                    nc.scalar.activation(l3_w[:, b, j, n * half:(n + 1) * half], tp_ps[n][:, 0:half], ACT.Copy
                                         ).then_inc(l3_ok, 1)

            def x3_high(b, c):
                for m in range(KD):
                    act.wait_ge(acc_out, (b * CH + c) * KD + m + 1)
                    nc.scalar.activation(x_hi[:, m, tokens(b, c)], x_f[:, m, tokens(b, c)], ACT.Copy
                                         ).then_inc(x3_hi, 1)

            def l2_pass(p, begins=None, last=False):
                for j in range(UPP):
                    for c in range(CH):
                        step(p * UPP * CH + j * CH + c, c, ACT.Gelu_apprx_tanh, 0.0)
                        s = j * CH + c
                        if begins is not None and s < L3U:
                            l3_evac(begins, s)
                            if 1 <= s <= CH:
                                x3_high(begins, s - 1)
                        if c == 0:
                            if j + 1 < UPP:
                                l2_dn(p, j + 1)
                            elif last:
                                l3_dn(0, 0)
                            else:
                                l2_dn(p + 1, 0)
                        elif j + 2 < UPP:
                            l2_gu(p, j + 2)
                        elif last:
                            l3_gu(0, j + 2 - UPP)
                        else:
                            l2_gu(p + 1, j + 2 - UPP)

            l2_pass(0)
            with act.Fori(1, PASSES) as p:
                l2_pass(p)
            l2_pass(PASSES, begins=0)
            for p in range(PASSES + 1, 2 * PASSES):
                l2_pass(p, last=p == 2 * PASSES - 1)

            def out_copy(b, c):
                act.wait_ge(out_tp[0], b * CH + c + 1)
                nc.scalar.activation(x_nat[:, b, c * TC:c * TC + 2, :].rearrange("p t d -> p (t d)"),
                                     tp_ps[0][:, :], ACT.Copy).then_inc(out_ok[0], 1)

            for b in range(B):
                act.wait_ge(s_bias[b], 48)
                for j in range(L3U):
                    for c in range(CH):
                        s = j * CH + c
                        step(CH * UNIT0[2 + b] + s, c, ACT.Silu, bu_col[:, b, j:j + 1])
                        if b == 0 and s < L3U:
                            l3_evac(1, s)
                            if 1 <= s <= CH:
                                x3_high(1, s - 1)
                        if b == 1 and 1 <= s <= CH:
                            out_copy(0, s - 1)
                        nb, nj = (b, j + 1 + c) if j + 1 + c < L3U else (b + 1, j + 1 + c - L3U)
                        if nb < B:
                            (l3_gu if c else l3_dn)(nb, nj)
            for c in range(CH):
                out_copy(1, c)

        @block.tensor
        def _(pe):
            pe.wait_ge(ident_ok, 1)
            pe.wait_ge(s_mask, 16)
            for k in range(KD):
                for o in range(KD):
                    mm = nc.tensor.transpose(tp_ps[1][:, k * D + o * P:k * D + (o + 1) * P],
                                             mask_nat[:, o, k * P:(k + 1) * P], ident[:, :])
            mm.then_inc(maskt_tp, 1)
            pe.wait_ge(s_bs, 32)
            for k in range(KD):
                mm = nc.tensor.transpose(tp_ps[0][:, k * P:(k + 1) * P],
                                         bs_nat[:, k, :, :].rearrange("p e r -> p (e r)"), ident[:, :])
            mm.then_inc(bst_tp, 1)

            pe.wait_ge(bst_ok, 1)
            pe.wait_ge(asw_ok, B)
            for k in range(KD):
                nc.tensor.matmul(banks[4 + k][:, :], bs_t[:, k * P:(k + 1) * P],
                                 as_w[:, :, :].rearrange("p b c -> p (b c)"), start=True, stop=True
                                 ).then_inc(w0_mm, 1)

            def xt(b):
                pe.wait_ge(s_x[b], 16)
                for n in range(4):
                    if b:
                        pe.wait_ge(xt_lo, n + 1)
                    k, c = n // 2, n % 2
                    for t in range(TC):
                        mm = nc.tensor.transpose(banks[n][:, t * P:(t + 1) * P],
                                                 x_nat[:, b, c * TC + t, k * P:(k + 1) * P], ident[:, :])
                    mm.then_inc(xt_tp, 1)

            pe.wait_ge(maskt_ok, 1)
            pe.wait_ge(diag_ok, B)
            for g in range(G):
                if g % 2 == 0:
                    pe.wait_ge(s_l1[g // 2], 16)
                for k in range(KD):
                    for o in range(KD):
                        mm = nc.tensor.matmul(
                            tp_ps[k][:, :].rearrange("p (b d) -> p b d", b=B)[:, :, o * P:(o + 1) * P],
                            l1_nat[:, g, o, k * P:(k + 1) * P], diag[:, g, :, :],
                            start=(g == 0 and o == 0), stop=(g == G - 1), skip_group_check=True)
                    if g == G - 1:
                        mm.then_inc(w1_mm, 1)
                if g == 3:
                    xt(0)
            pe.wait_ge(w0_ok, KD * B)
            for b in range(B):
                if b == 0:
                    pe.wait_ge(w1_ok, KD * B)
                for cb in range(KD):
                    for k in range(KD):
                        mm = nc.tensor.matmul(banks[4 + b][:, cb * D:(cb + 1) * D],
                                              w0i[:, k, b, cb * P:(cb + 1) * P], w1it[:, k, b, :],
                                              start=(k == 0), stop=(k == KD - 1), skip_group_check=True)
                mm.then_inc(m_mm, 1)
            pe.wait_ge(s_b0, 16)
            for b in range(B):
                for m in range(KD):
                    for k in range(KD):
                        mm = nc.tensor.matmul(banks[6][:, b * KD + m:b * KD + m + 1],
                                              w1it[:, k, b, m * P:(m + 1) * P], b0_col[:, k:k + 1],
                                              start=(k == 0), stop=(k == KD - 1), skip_group_check=True)
            mm.then_inc(be_mm, 1)
            xt(1)

            for b in range(B):
                pe.wait_ge(xt_lo, 4 * b + 4)
                pe.wait_ge(mlo_ok, B)
                for c in range(CH):
                    if b == 0 and c == 1:
                        pe.wait_ge(be_ok, 1)
                    for m in range(KD):
                        n = 0
                        for k in range(KD):
                            for w, y in ((m_lo, x_hi), (m_hi, x_hi), (m_hi, x_lo)):
                                mm = nc.tensor.matmul(x2_bank(b, c, m)[:, :], w[:, b, k, m * P:(m + 1) * P],
                                                      y[:, k, tokens(b, c)], start=(n == 0),
                                                      stop=(n == 3 * KD - 1))
                                n += 1
                        mm.then_inc(x2_mm, 1)

            def gate_up(s, slot, b, c):
                for a, bank, free, made in ((0, act_ps, g_ok, act_mm), (1, lin_ps, h_ok, lin_mm)):
                    if not isinstance(s, int) or s >= 1:
                        pe.wait_ge(free, s)
                    n = 0
                    for k in range(KD):
                        for w, y in ((gu_lo, x_hi), (gu_hi, x_hi), (gu_hi, x_lo)):
                            mm = nc.tensor.matmul(bank[:, :], w[:, slot, a * KD + k, :], y[:, k, tokens(b, c)],
                                                  start=(n == 0), stop=(n == 3 * KD - 1))
                            n += 1
                    mm.then_inc(made, 1)

            def down(s, u, slot, c, start, stop):
                pe.wait_ge(dnlo_ok, u + 1)
                pe.wait_ge(hhi_ok, s + 1)
                for m in range(KD):
                    for w in (dn_lo, dn_hi):
                        nc.tensor.matmul(acc[2 * m + c][:, :], w[:, slot, m * P:(m + 1) * P], h_hi[:, c, :],
                                         start=start and w is dn_lo, stop=False, skip_group_check=True)
                pe.wait_ge(hlo_ok, s + 1)
                for m in range(KD):
                    mm = nc.tensor.matmul(acc[2 * m + c][:, :], dn_hi[:, slot, m * P:(m + 1) * P], h_lo[:, c, :],
                                          start=False, stop=stop, skip_group_check=True)
                mm.then_inc(down_mm, 1)

            def two_units(u, b, group=None, last=False, hook=None):
                for i in range(2 * CH):
                    s = u * CH + i
                    if i % CH == 0:
                        pe.wait_ge(gulo_ok, u + i // CH + 1)
                    if group is not None and i < CH:
                        if group == 0:
                            pe.wait_ge(x2_lo, KD * (i + 1))
                        elif group == 1:
                            pe.wait_ge(x2_lo, KD * (CH + i + 1))
                        else:
                            pe.wait_ge(x3_lo, KD * (CH * b + i + 1))
                    gate_up(s, i // CH, b, i % CH)
                    if not (group == 0 and i == 0):
                        if group is not None and group > 0 and 1 <= i <= CH:
                            pe.wait_ge(acc_out, KD * (CH * (group - 1) + i))
                        if group == 0 and i == 1:
                            pe.wait_ge(x2_f, KD * CH * B)
                        down_slot = ((i - 1) // CH) % 2
                        down(s - 1, u + (i - 1) // CH, down_slot, (i - 1) % CH,
                             group is not None and 1 <= i <= CH,
                             (group is not None and group > 0 and i == 0) or (last and i == 2 * CH - 1))
                    if hook:
                        hook(i)

            def l3_transposes(b, j):
                if j == 0:
                    pe.wait_ge(s_l3[b], 48)
                blocks = [l3_ug[:, b, a, j, k * P:(k + 1) * P] for a in range(2) for k in range(KD)]
                blocks += [l3_dn[:, b, m, j * P:(j + 1) * P] for m in range(KD)]
                for n in range(2):
                    if b or j:
                        pe.wait_ge(l3_ok, 2 * (b * L3U + j) + n - 1)
                    for i in range(3):
                        mm = nc.tensor.transpose(tp_ps[n][:, i * P:(i + 1) * P], blocks[3 * n + i], ident[:, :])
                    mm.then_inc(l3_tp, 1)

            def out_transposes(b, c):
                pe.wait_ge(acc_out, KD * (CH * (B + b) + c + 1))
                for n in range(2):
                    if b * CH + c:
                        pe.wait_ge(out_ok[n], b * CH + c)
                    else:
                        pe.wait_ge(l3_ok, 2 * B * L3U)
                    for i in range(2):
                        t0 = b * T + (c * TC + 2 * n + i) * P
                        for m in range(KD):
                            mm = nc.tensor.transpose(tp_ps[n][:, i * D + m * P:i * D + (m + 1) * P],
                                                     x_f[:, m, t0:t0 + P], ident[:, :])
                    mm.then_inc(out_tp[n], 1)

            for b in range(B):
                u0 = UNIT0[b]
                two_units(u0, b, group=b, hook=(lambda i: l3_transposes(0, i)) if b else None)
                with pe.Fori(u0 + 2, u0 + G2U, 2) as u:
                    two_units(u, b)
            for b in range(B):
                u0 = UNIT0[B + b]
                two_units(u0, b, group=B + b,
                          hook=(lambda i: l3_transposes(1, i)) if b == 0 else
                          (lambda i: out_transposes(0, i - 1) if 1 <= i <= CH else None))
                two_units(u0 + 2, b, last=True)
            out_transposes(1, 0)
            down(END[3] - 1, UNIT0[4] - 1, 1, CH - 1, False, True)
            out_transposes(1, 1)

        @block.vector
        def _(dve):
            dve.wait_ge(ident_ok, 1)
            dve.wait_ge(s_cond, 16)
            for b in range(B):
                for g in range(G):
                    ins = nc.vector.tensor_scalar(diag[:, g, b, :], ident[:, :], cond_r[:, b, g:g + 1], None, ALU.mult)
                ins.then_inc(diag_ok, 1)
            for b in range(B):
                nc.vector.max(top_v[:, b, :], cond_r[:, b, :]).then_inc(r_max, 1)
                dve.wait_ge(r_max, b + 1)
                nc.vector.max_index(top_i[:, b, :], top_v[:, b, :], cond_r[:, b, :]).then_inc(r_idx, 1)
                nc.vector.tensor_scalar(neg_m[:, b:b + 1], top_v[:, b, 0:1], -1.0, None, ALU.mult).then_inc(r_neg, 1)
            dve.wait_ge(s_as, 16)
            dve.wait_ge(s_er, 32)
            for b in range(B):
                nc.vector.tensor_scalar(as_w[:, b, :], as_nat[:, :], cond_er[:, b:b + 1], LORA_SCALING,
                                        ALU.mult, ALU.mult).then_inc(asw_ok, 1)
            dve.wait_ge(s_wb, 16)
            for k in range(KD):
                nc.vector.tensor_tensor(wb[:, k, k * P:(k + 1) * P], wb[:, k, k * P:(k + 1) * P], ident[:, :],
                                        ALU.add).then_inc(wbi_ok, 1)
            dve.wait_ge(wbi_ok, KD)
            for k in range(KD):
                dve.wait_ge(w0_mm, k + 1)
                for b in range(B):
                    nc.vector.tensor_tensor(w0i[:, k, b, :], banks[4 + k][:, b * D:(b + 1) * D], wb[:, k, :],
                                            ALU.add).then_inc(w0_ok, 1)

            def xt_low(b):
                for n in range(4):
                    dve.wait_ge(xt_hi, 4 * b + n + 1)
                    nc.vector.tensor_tensor(x_lo[:, n // 2, tokens(b, n % 2)], banks[n][:, :],
                                            x_hi[:, n // 2, tokens(b, n % 2)].bitcast(F32),
                                            ALU.subtract).then_inc(xt_lo, 1)

            dve.wait_ge(r_exp, B)
            nc.vector.reciprocal(r_inv[:, :], r_sum[:, :]).then_inc(r_inv_ok, 1)
            dve.wait_ge(r_inv_ok, 1)
            for b in range(B):
                nc.vector.tensor_scalar(top_p[:, b, :], top_e[:, b, 0:2], r_inv[:, b:b + 1], None, ALU.mult
                                        ).then_inc(r_p, 1)
            dve.wait_ge(r_p, B)
            nc.vector.tensor_tensor(r_sum[:, :], top_p[:, :, 0], top_p[:, :, 1], ALU.add).then_inc(r_s2, 1)
            dve.wait_ge(r_s2, 1)
            nc.vector.reciprocal(r_inv[:, :], r_sum[:, :]).then_inc(r_inv_ok, 1)
            dve.wait_ge(r_inv_ok, 2)
            nc.vector.memset(w_pass[:, :, 0:1], 1.0).then_inc(r_w, 1)
            for b in range(B):
                nc.vector.tensor_scalar(w_raw[:, b, :], top_p[:, b, :], r_inv[:, b:b + 1], None, ALU.mult
                                        ).then_inc(r_w, 1)
            dve.wait_ge(r_w, 1 + B)
            nc.vector.tensor_scalar(w_part[:, :, :], w_raw[:, :, :], 1.0 - MOE_SCALE, None, ALU.mult).then_inc(r_w, 1)
            dve.wait_ge(r_w, 2 + B)
            nc.vector.scalar_tensor_tensor(out=w_pass[:, :, 1:PASSES], in0=w_raw[:, :, :], scalar=MOE_SCALE,
                                           in1=w_part[:, :, :], op0=ALU.mult, op1=ALU.add).then_inc(r_w, 1)

            xt_low(0)
            for k in range(KD):
                dve.wait_ge(w1_mm, k + 1)
                for b in range(B):
                    nc.vector.tensor_tensor(w1it[:, k, b, :], tp_ps[k][:, b * D:(b + 1) * D], mask_t[:, k, :],
                                            ALU.mult).then_inc(w1_masked, 1)
            for k in range(KD):
                for b in range(B):
                    dve.wait_ge(w1_masked, k * B + b + 1)
                    nc.vector.tensor_tensor(w1it[:, k, b, k * P:(k + 1) * P], w1it[:, k, b, k * P:(k + 1) * P],
                                            ident[:, :], ALU.add).then_inc(w1_ok, 1)
            for b in range(B):
                dve.wait_ge(mhi_ok, b + 1)
                nc.vector.tensor_tensor(m_lo[:, b, :, :].rearrange("p k d -> p (k d)"), banks[4 + b][:, :],
                                        m_hi[:, b, :, :].rearrange("p k d -> p (k d)").bitcast(F32),
                                        ALU.subtract).then_inc(mlo_ok, 1)
            dve.wait_ge(be_mm, 1)
            dve.wait_ge(s_b1, 16)
            for b in range(B):
                ins = nc.vector.tensor_tensor(b_eff[:, b, :], banks[6][:, b * KD:(b + 1) * KD], b1_col[:, :], ALU.add)
            ins.then_inc(be_ok, 1)
            xt_low(1)
            dve.wait_ge(be_ok, 1)
            for b in range(B):
                for c in range(CH):
                    dve.wait_ge(x2_mm, (b * CH + c + 1) * KD)
                    for m in range(KD):
                        nc.vector.tensor_scalar(x_f[:, m, tokens(b, c)], x2_bank(b, c, m)[:, :],
                                                b_eff[:, b, m:m + 1], None, ALU.add).then_inc(x2_f, 1)
                    for m in range(KD):
                        dve.wait_ge(x2_hi, (b * CH + c) * KD + m + 1)
                        nc.vector.tensor_tensor(x_lo[:, m, tokens(b, c)], x_f[:, m, tokens(b, c)],
                                                x_hi[:, m, tokens(b, c)].bitcast(F32),
                                                ALU.subtract).then_inc(x2_lo, 1)

            def step(s, c, layer, w):
                dve.wait_ge(lin_mm, s + 1)
                dve.wait_ge(g_ok, s + 1)
                if layer == 2:
                    nc.vector.scalar_tensor_tensor(out=h_f[:, c, :], in0=g_f[:, c, :], scalar=w, in1=lin_ps[:, :],
                                                   op0=ALU.mult, op1=ALU.mult).then_inc(h_ok, 1)
                else:
                    nc.vector.scalar_tensor_tensor(out=h_f[:, c, :], in0=lin_ps[:, :], scalar=w, in1=g_f[:, c, :],
                                                   op0=ALU.add, op1=ALU.mult).then_inc(h_ok, 1)
                dve.wait_ge(hhi_ok, s + 1)
                nc.vector.tensor_tensor(h_lo[:, c, :], h_f[:, c, :], h_hi[:, c, :].bitcast(F32), ALU.subtract
                                        ).then_inc(hlo_ok, 1)

            def take(group, b, c):
                dve.wait_ge(down_mm, END[group] - 1 + c)
                for m in range(KD):
                    if group < B:
                        nc.vector.tensor_tensor(x_f[:, m, tokens(b, c)], acc[2 * m + c][:, :],
                                                x_f[:, m, tokens(b, c)], ALU.add).then_inc(acc_out, 1)
                    else:
                        nc.vector.scalar_tensor_tensor(out=x_f[:, m, tokens(b, c)], in0=acc[2 * m + c][:, :],
                                                       scalar=bd_col[:, b, m:m + 1], in1=x_f[:, m, tokens(b, c)],
                                                       op0=ALU.add, op1=ALU.add).then_inc(acc_out, 1)

            def out_copy(b, c):
                dve.wait_ge(out_tp[1], b * CH + c + 1)
                nc.vector.tensor_copy(x_nat[:, b, c * TC + 2:c * TC + 4, :].rearrange("p t d -> p (t d)"),
                                      tp_ps[1][:, :]).then_inc(out_ok[1], 1)

            def l2_units(b, p, first):
                with dve.Fori(first, UPP) as j:
                    for c in range(CH):
                        step((b * PASSES + p) * UPP * CH + j * CH + c, c, 2, w_pass[:, b, bass.ds(p, 1)])

            dve.wait_ge(r_w, 3 + B)
            with dve.Fori(0, PASSES) as p:
                l2_units(0, p, 0)
            for c in range(CH):
                take(0, 0, c)
                step(END[0] + c, c, 2, w_pass[:, 1, 0:1])
            l2_units(1, 0, 1)
            with dve.Fori(1, PASSES) as p:
                l2_units(1, p, 0)
            for b in range(B):
                dve.wait_ge(s_bias[b], 48)
                for j in range(L3U):
                    for c in range(CH):
                        if j == 0:
                            take(1 + b, 1 - b, c)
                        step(CH * UNIT0[2 + b] + j * CH + c, c, 3, bg_col[:, b, j:j + 1])
                        if b == 1 and 1 <= j * CH + c <= CH:
                            out_copy(0, j * CH + c - 1)
            for c in range(CH):
                take(3, 1, c)
            for c in range(CH):
                out_copy(1, c)


_INS = ['x', 'cond_8', 'L0_cond_W_base', 'L0_cond_b_base', 'L0_cond_As', 'L0_cond_Bs', 'L1_cond_weight',
        'L1_cond_mask', 'L1_cond_bias', 'L2_cond_skill_gate', 'L2_cond_skill_up', 'L2_cond_skill_down',
        'L2_cond_shared_gate', 'L2_cond_shared_up', 'L2_cond_shared_down', 'L3_cond_W_up', 'L3_cond_b_up',
        'L3_cond_W_gate', 'L3_cond_b_gate', 'L3_cond_W_down', 'L3_cond_b_down']


def kernel(**inputs):
    import numpy as _np
    import concourse.bacc as _bacc
    from concourse import mybir as _mybir
    from concourse.bass_utils import run_bass_kernel_spmd as _run

    nc = _bacc.Bacc("TRN2", target_bir_lowering=False, num_devices=1)
    arrays, args = {}, []
    for name in _INS:
        a = _np.ascontiguousarray(inputs[name])
        arrays[f"in_{name}_dram"] = a
        args.append(nc.dram_tensor(f"in_{name}_dram", a.shape, _mybir.dt.from_np(a.dtype), kind="ExternalInput").ap())
    x = inputs['x']
    args.append(nc.dram_tensor("out_dram", x.shape, _mybir.dt.from_np(_np.dtype(x.dtype)), kind="ExternalOutput").ap())
    cond_residual_stack(nc, *args)
    r = _run(nc, [arrays], core_ids=[0])
    return r.results[0]["out_dram"]
```

```python
from contextlib import ExitStack

import concourse.bass as bass
from concourse import mybir

F32 = mybir.dt.float32
F32R = mybir.dt.float32r
U32 = mybir.dt.uint32
ALU = mybir.AluOpType
ACT = mybir.ActivationFunctionType

P = 128
MOVE = 512
LORA_SCALING = 32.0 / 16.0
MOE_SCALE = 1.0 / 12.0


def cond_residual_stack(nc, x, cond, w_base, b_base, lora_a, lora_b, l1_w, l1_mask, l1_bias,
                        moe_gate, moe_up, moe_down, sh_gate, sh_up, sh_down,
                        w_up, b_up, w_gate, b_gate, w_down, b_down, out):
    B, T, D = x.shape
    G = cond.shape[1]
    R = lora_a.shape[1]
    KD = D // P
    TB = T // P
    CH = T // MOVE
    TC = MOVE // P
    UPQ = 4
    QW = UPQ * P
    QPP = moe_gate.shape[2] // QW
    UPP = QPP * UPQ
    PASSES = 3
    L3U = w_up.shape[1] // P
    G2U = PASSES * UPP
    UNIT0 = [0, G2U, 2 * G2U, 2 * G2U + L3U, 2 * G2U + 2 * L3U]
    END = [CH * u for u in UNIT0[1:]]
    assert (KD, CH, B, L3U, QPP, G * R) == (2, 2, 2, UPQ, 2, P)
    SLOT = 3 * 16

    x_t = x.rearrange("b (t p) d -> p b t d", p=P)
    out_t = out.rearrange("b (t p) d -> p b t d", p=P)

    with ExitStack() as ctx:
        def sb(name, shape, dt=F32):
            return ctx.enter_context(nc.sbuf_tensor(name, shape, dt))

        def sem(name):
            return ctx.enter_context(nc.semaphore(name))

        x_f = sb("x_f", [P, KD, B * T])
        x_hi = sb("x_hi", [P, KD, B * T], F32R)
        x_lo = sb("x_lo", [P, KD, B * T], F32R)
        x_nat = sb("x_nat", [P, B, TB, D])
        g_f = sb("g_f", [P, 2, MOVE])
        h_f = sb("h_f", [P, 2, MOVE])
        h_hi = sb("h_hi", [P, 2, MOVE], F32R)
        h_lo = sb("h_lo", [P, 2, MOVE], F32R)
        raw_gu = sb("raw_gu", [P, QPP, 2, KD, QW])
        raw_dn = sb("raw_dn", [P, QPP, UPQ, D])
        gu_hi = sb("gu_hi", [P, 2, 2 * KD, P], F32R)
        gu_lo = sb("gu_lo", [P, 2, 2 * KD, P], F32R)
        dn_hi = sb("dn_hi", [P, 2, D], F32R)
        dn_lo = sb("dn_lo", [P, 2, D], F32R)
        l3_w = sb("l3_w", [P, B, L3U, 2 * KD * P + D])
        l1_nat = sb("l1_nat", [P, G, KD, D])
        diag = sb("diag", [P, G, P])
        w1_nat = sb("w1_nat", [P, KD, D])
        l3_ug = l1_nat[:, :, :, :].rearrange("p (b a h) k d -> p b a (h k) d", b=B, a=2)
        l3_dn = sb("l3_dn", [P, B, KD, L3U * P])
        ident = sb("ident", [P, P])
        bs_nat = sb("bs_nat", [P, KD, G, R])
        bs_t = sb("bs_t", [P, D])
        as_nat = sb("as_nat", [P, D])
        as_w = sb("as_w", [P, B, D])
        wb = sb("wb", [P, KD, D])
        mask_nat = sb("mask_nat", [P, KD, D])
        mask_t = sb("mask_t", [P, KD, D])
        w0i = sb("w0i", [P, KD, B, D])
        w1it = sb("w1it", [P, KD, B, D])
        m_hi = sb("m_hi", [P, B, KD, D], F32R)
        m_lo = sb("m_lo", [P, B, KD, D], F32R)
        b0_col = sb("b0_col", [P, KD])
        b1_col = sb("b1_col", [P, KD])
        b_eff = sb("b_eff", [P, B, KD])
        cond_r = sb("cond_r", [P, B, G])
        cond_er = sb("cond_er", [P, B])
        lora_s = sb("lora_s", [P, B])
        top_v = sb("top_v", [P, B, 8])
        top_i = sb("top_i", [P, B, 8], U32)
        neg_m = sb("neg_m", [P, B])
        top_e = sb("top_e", [P, B, 8])
        r_sum = sb("r_sum", [P, B])
        r_inv = sb("r_inv", [P, B])
        top_p = sb("top_p", [P, B, 2])
        w_raw = sb("w_raw", [P, B, 2])
        w_part = sb("w_part", [P, B, 2])
        w_pass = sb("w_pass", [P, B, PASSES])
        bu_col = sb("bu_col", [P, B, L3U])
        bg_col = sb("bg_col", [P, B, L3U])
        bd_col = sb("bd_col", [P, B, KD])

        banks = [ctx.enter_context(nc.psum_tensor(f"bank{n}", [P, MOVE], F32)) for n in range(8)]
        acc = banks[0:4]
        act_ps, lin_ps = banks[4], banks[5]
        tp_ps = banks[6:8]

        s_cond, s_er, s_bs, s_as, s_wb, s_mask, s_b0, s_b1 = (
            sem(n) for n in ("cond_in", "er_in", "bs_in", "as_in", "wb_in", "mask_in", "b0_in", "b1_in"))
        s_x = [[sem(f"x_in{b}{c}") for c in range(CH)] for b in range(B)]
        s_l1 = [sem(f"l1_in{n}") for n in range(G // 2)]
        s_raw = [sem(f"raw_in{n}") for n in range(QPP)]
        s_l3 = [sem(f"l3_in{b}") for b in range(B)]
        s_bias = [sem(f"l3_bias_in{b}") for b in range(B)]
        zeroed, ident_ok, diag_ok, wbi_ok, loras_ok, asw_ok = (
            sem(n) for n in ("zeroed", "ident_ok", "diag_ok", "wbi_ok", "loras_ok", "asw_ok"))
        w1n_sum, w1n_masked, w1n_ok, w1t_tp = (sem(n) for n in ("w1n_sum", "w1n_masked", "w1n_ok", "w1t_tp"))
        bst_tp, bst_ok, maskt_tp, maskt_ok = (sem(n) for n in ("bst_tp", "bst_ok", "maskt_tp", "maskt_ok"))
        xt_tp, xt_hi, xt_lo = (sem(n) for n in ("xt_tp", "xt_hi", "xt_lo"))
        w0_mm, w0_ok, w1_mm, w1_masked, w1_ok, w1b_ok, warm = (
            sem(n) for n in ("w0_mm", "w0_ok", "w1_mm", "w1_masked", "w1_ok", "w1b_ok", "warm"))
        m_mm, mhi_ok, mlo_ok, be_mm, be_ok = (sem(n) for n in ("m_mm", "mhi_ok", "mlo_ok", "be_mm", "be_ok"))
        x2_mm, x2_f, x2_hi, x2_lo = (sem(n) for n in ("x2_mm", "x2_f", "x2_hi", "x2_lo"))
        r_max, r_idx, r_neg, r_exp, r_inv_ok, r_p, r_s2, r_w = (
            sem(n) for n in ("r_max", "r_idx", "r_neg", "r_exp", "r_inv_ok", "r_p", "r_s2", "r_w"))
        guhi_ok, gulo_ok, dnhi_ok, dnlo_ok = (sem(n) for n in ("guhi_ok", "gulo_ok", "dnhi_ok", "dnlo_ok"))
        act_mm, lin_mm, g_ok, h_ok, hhi_ok, hlo_ok, down_mm = (
            sem(n) for n in ("act_mm", "lin_mm", "g_ok", "h_ok", "hhi_ok", "hlo_ok", "down_mm"))
        acc_out = sem("acc_out")
        x3_hi, x3_lo = sem("x3_hi"), sem("x3_lo")
        l3_tp, l3_ok = sem("l3_tp"), sem("l3_ok")
        out_tp = [sem(f"out_tp{n}") for n in range(2)]
        out_ok = [sem(f"out_ok{n}") for n in range(2)]
        stored = sem("stored")

        block = ctx.enter_context(nc.Block())

        def tokens(b, c):
            return slice(b * T + c * MOVE, b * T + (c + 1) * MOVE)

        def xt_bank(b, c, k):
            return banks[2 * k + c] if b == 0 else tp_ps[k]

        x2_bank = xt_bank

        def m_bank(b):
            return banks[5] if b == 0 else tp_ps[0]

        def be_bank(b):
            return banks[4] if b == 0 else tp_ps[1]

        def l2_unit(j):
            return j // UPQ, j % UPQ

        @block.sync
        def _(sp):
            sp.dma_start(cond_r[:, :, :], bass.AP(cond.tensor, 0, [[0, P], [G, B], [1, G]])).then_inc(s_cond, 16)

            def load_l1(n):
                sp.dma_start(l1_nat[:, 2 * n:2 * n + 2, :, :].rearrange("p g k d -> p (g k) d"),
                             l1_w[2 * n:2 * n + 2, :, :].rearrange("g (k p) d -> p (g k) d", p=P)
                             ).then_inc(s_l1[n], 16)

            def load_x(b, c):
                sp.dma_start(x_nat[:, b, c * TC:(c + 1) * TC, :], x_t[:, b, c * TC:(c + 1) * TC, :]
                             ).then_inc(s_x[b][c], 16)

            load_l1(0)
            for k in range(KD):
                sp.dma_start(bs_nat[:, k, :, :], lora_b[:, k * P:(k + 1) * P, :].rearrange("e p r -> p e r")
                             ).then_inc(s_bs, 16)
            load_l1(1)
            with nc.allow_non_contiguous_dma(reason="columns"):
                for b in range(B):
                    sp.dma_start(cond_er[:, b:b + 1], bass.AP(cond.tensor, b * G, [[1, G], [0, R], [1, 1]])
                                 ).then_inc(s_er, 16)
            sp.dma_start(as_nat[:, :], lora_a.rearrange("e r c -> (e r) c")).then_inc(s_as, 16)
            load_l1(2)
            load_l1(3)
            sp.dma_start(mask_nat[:, :, :], l1_mask.rearrange("(k p) d -> p k d", p=P)).then_inc(s_mask, 16)
            sp.dma_start(wb[:, :, :], w_base.rearrange("(k p) d -> p k d", p=P)).then_inc(s_wb, 16)
            load_x(0, 0)
            load_x(0, 1)
            with nc.allow_non_contiguous_dma(reason="columns"):
                sp.dma_start(b0_col[:, :], b_base.rearrange("(k p) -> p k", p=P)).then_inc(s_b0, 16)
                sp.dma_start(b1_col[:, :], l1_bias.rearrange("(k p) -> p k", p=P)).then_inc(s_b1, 16)

            def load_quad(slot, gate, up, down):
                cols = slice(slot * QW, (slot + 1) * QW)
                for a, w in ((0, gate), (1, up)):
                    sp.dma_start(raw_gu[:, slot, a, :, :],
                                 w[:, cols].rearrange("(k p) c -> p k c", p=P)).then_inc(s_raw[slot], 16)
                sp.dma_start(raw_dn[:, slot, :, :],
                             down[cols, :].rearrange("(j p) d -> p j d", p=P)).then_inc(s_raw[slot], 16)

            for slot in range(QPP):
                load_quad(slot, sh_gate, sh_up, sh_down)
            for c in range(CH):
                load_x(1, c)

            def load_l3(b):
                e = sp.value_load(top_i[0:1, b, 0:1], min_val=0, max_val=G - 1)
                for a, w in ((0, w_up), (1, w_gate)):
                    sp.dma_start(l3_ug[:, b, a, :, :],
                                 w[bass.ds(e, 1), :, :].rearrange("o (j p) d -> p (o j) d", p=P)
                                 ).then_inc(s_l3[b], 16)
                sp.dma_start(l3_dn[:, b, :, :],
                             w_down[bass.ds(e, 1), :, :].rearrange("o (m p) h -> p (o m) h", p=P)
                             ).then_inc(s_l3[b], 16)
                with nc.allow_non_contiguous_dma(reason="bias columns"):
                    for col, v in ((bu_col, b_up), (bg_col, b_gate), (bd_col, b_down)):
                        sp.dma_start(col[:, b, :], v[bass.ds(e, 1), :].rearrange("o (j p) -> p (o j)", p=P)
                                     ).then_inc(s_bias[b], 16)

            sp.wait_ge(r_idx, B)
            sp.wait_ge(w1n_sum, G)
            sp.wait_ge(w1_mm, KD)
            for b in range(B):
                load_l3(b)

            def freed(q):
                sp.wait_ge(gulo_ok, (q - QPP + 1) * UPQ)
                sp.wait_ge(dnlo_ok, (q - QPP + 1) * UPQ)

            for b in range(B):
                if b:
                    for slot in range(QPP):
                        freed(b * PASSES * QPP + slot)
                        load_quad(slot, sh_gate, sh_up, sh_down)
                with sp.Fori(0, PASSES - 1) as k:
                    e = sp.value_load(top_i[0:1, b, bass.ds(k, 1)], min_val=0, max_val=G - 1)
                    for slot in range(QPP):
                        freed(k * QPP + (b * PASSES + 1) * QPP + slot)
                        cols = slice(slot * QW, (slot + 1) * QW)
                        for a, w in ((0, moe_gate), (1, moe_up)):
                            sp.dma_start(raw_gu[:, slot, a, :, :],
                                         w[bass.ds(e, 1), :, cols].rearrange("o (k p) c -> p (o k) c", p=P)
                                         ).then_inc(s_raw[slot], 16)
                        sp.dma_start(raw_dn[:, slot, :, :],
                                     moe_down[bass.ds(e, 1), cols, :].rearrange("o (j p) d -> p (o j) d", p=P)
                                     ).then_inc(s_raw[slot], 16)

            for b in range(B):
                for c in range(CH):
                    for n in range(2):
                        sp.wait_ge(out_ok[n], b * CH + c + 1)
                        t0 = c * TC + 2 * n
                        sp.dma_start(out_t[:, b, t0:t0 + 2, :], x_nat[:, b, t0:t0 + 2, :]).then_inc(stored, 16)
            sp.wait_ge(stored, 16 * B * CH * 2)

        @block.gpsimd
        def _(pool):
            nc.gpsimd.memset(ident[:, :], 0.0).then_inc(zeroed, 1)
            pool.wait_ge(zeroed, 1)
            nc.gpsimd.affine_select(out=ident[:, :], in_=ident[:, :], compare_op=ALU.not_equal, fill=1.0,
                                    base=0, pattern=[[-1, P]], channel_multiplier=1).then_inc(ident_ok, 1)

            def split_lo(v, slot, gu_src, dn_src):
                pool.wait_ge(guhi_ok, v + 1)
                nc.gpsimd.tensor_tensor(gu_lo[:, slot, :, :], gu_src, gu_hi[:, slot, :, :].bitcast(F32),
                                        ALU.subtract).then_inc(gulo_ok, 1)
                pool.wait_ge(dnhi_ok, v + 1)
                nc.gpsimd.tensor_tensor(dn_lo[:, slot, :], dn_src, dn_hi[:, slot, :].bitcast(F32),
                                        ALU.subtract).then_inc(dnlo_ok, 1)

            def x3_low(b):
                for c in range(CH):
                    for m in range(KD):
                        pool.wait_ge(x3_hi, (b * CH + c) * KD + m + 1)
                        nc.gpsimd.tensor_tensor(x_lo[:, m, tokens(b, c)], x_f[:, m, tokens(b, c)],
                                                x_hi[:, m, tokens(b, c)].bitcast(F32),
                                                ALU.subtract).then_inc(x3_lo, 1)

            def l2_passes(first, last):
                with pool.Fori(first, last) as p:
                    for q in range(QPP):
                        for j in range(UPQ):
                            split_lo(p * UPP + q * UPQ + j, j % 2,
                                     raw_gu[:, q, :, :, j * P:(j + 1) * P].rearrange("p a k c -> p (a k) c"),
                                     raw_dn[:, q, j, :])

            l2_passes(0, PASSES + 1)
            x3_low(0)
            l2_passes(PASSES + 1, 2 * PASSES)
            for b in range(B):
                for j in range(L3U):
                    split_lo(UNIT0[2 + b] + j, j % 2,
                             l3_w[:, b, j, 0:2 * KD * P].rearrange("p (a c) -> p a c", c=P),
                             l3_w[:, b, j, 2 * KD * P:])
                    if b == 0 and j == 2:
                        x3_low(1)

        @block.scalar
        def _(act):
            act.wait_ge(ident_ok, 1)
            act.wait_ge(s_cond, 16)
            for g in range(G):
                nc.scalar.activation(diag[:, g, :], ident[:, :], ACT.Copy, scale=cond_r[:, 1, g:g + 1]
                                     ).then_inc(diag_ok, 1)
            for b in range(B):
                act.wait_ge(r_neg, b + 1)
                nc.scalar.activation(top_e[:, b, :], top_v[:, b, :], ACT.Exp, bias=neg_m[:, b:b + 1],
                                     accum_out=r_sum[:, b:b + 1]).then_inc(r_exp, 1)
            nc.scalar.activation(g_f[:, 0, 0:8], top_v[:, 0, :], ACT.Gelu_apprx_tanh).then_inc(warm, 1)

            act.wait_ge(s_er, 32)
            nc.scalar.activation(lora_s[:, :], cond_er[:, :], ACT.Copy, scale=LORA_SCALING).then_inc(loras_ok, 1)
            act.wait_ge(loras_ok, 1)
            act.wait_ge(s_as, 16)
            for b in range(B):
                nc.scalar.activation(as_w[:, b, :], as_nat[:, :], ACT.Copy, scale=lora_s[:, b:b + 1]
                                     ).then_inc(asw_ok, 1)
            act.wait_ge(bst_tp, 1)
            nc.scalar.activation(bs_t[:, :], banks[5][:, 0:D], ACT.Copy).then_inc(bst_ok, 1)
            act.wait_ge(maskt_tp, 1)
            nc.scalar.activation(mask_t[:, :, :].rearrange("p k d -> p (k d)"), banks[4][:, :], ACT.Copy
                                 ).then_inc(maskt_ok, 1)

            def xt_high(b, c):
                for k in range(KD):
                    act.wait_ge(xt_tp, (b * CH + c) * KD + k + 1)
                    nc.scalar.activation(x_hi[:, k, tokens(b, c)], xt_bank(b, c, k)[:, :], ACT.Copy
                                         ).then_inc(xt_hi, 1)

            def m_high(b):
                act.wait_ge(m_mm, b + 1)
                nc.scalar.activation(m_hi[:, b, :, :], m_bank(b)[:, :].rearrange("p (k d) -> p k d", k=KD),
                                     ACT.Copy).then_inc(mhi_ok, 1)

            def x2_high(b, c):
                for m in range(KD):
                    act.wait_ge(x2_f, (b * CH + c) * KD + m + 1)
                    nc.scalar.activation(x_hi[:, m, tokens(b, c)], x_f[:, m, tokens(b, c)], ACT.Copy
                                         ).then_inc(x2_hi, 1)

            xt_high(0, 0)
            act.wait_ge(w1t_tp, 1)
            nc.scalar.activation(w1it[:, :, 0, :], banks[4][:, :].rearrange("p (k d) -> p k d", k=KD), ACT.Copy
                                 ).then_inc(w1_ok, 1)
            xt_high(0, 1)

            def split_gu(v, slot, src, loaded, count):
                act.wait_ge(loaded, count)
                if not isinstance(v, int) or v >= 2:
                    act.wait_ge(lin_mm, CH * v - CH)
                nc.scalar.activation(gu_hi[:, slot, :, :], src, ACT.Copy).then_inc(guhi_ok, 1)

            def split_dn(v, slot, src, loaded, count):
                act.wait_ge(loaded, count)
                if not isinstance(v, int) or v >= 2:
                    act.wait_ge(down_mm, CH * v - CH)
                nc.scalar.activation(dn_hi[:, slot, :], src, ACT.Copy).then_inc(dnhi_ok, 1)

            def l2_gu(p, j):
                q, u = l2_unit(j)
                split_gu(p * UPP + j, j % 2, raw_gu[:, q, :, :, u * P:(u + 1) * P].rearrange("p a k c -> p (a k) c"),
                         s_raw[q], p * SLOT + SLOT)

            def l2_dn(p, j):
                q, u = l2_unit(j)
                split_dn(p * UPP + j, j % 2, raw_dn[:, q, u, :], s_raw[q], p * SLOT + SLOT)

            def l3_gu(b, j):
                split_gu(UNIT0[2 + b] + j, j % 2,
                         l3_w[:, b, j, 0:2 * KD * P].rearrange("p (a c) -> p a c", c=P),
                         l3_ok, 2 * (b * L3U + j) + 2)

            def l3_dn(b, j):
                split_dn(UNIT0[2 + b] + j, j % 2, l3_w[:, b, j, 2 * KD * P:], l3_ok, 2 * (b * L3U + j) + 2)

            m_high(0)
            l2_gu(0, 0)
            l2_dn(0, 0)
            x2_high(0, 0)
            l2_gu(0, 1)
            x2_high(0, 1)
            start = [lambda: m_high(1), lambda: xt_high(1, 0), lambda: xt_high(1, 1),
                     lambda: x2_high(1, 0), lambda: x2_high(1, 1)]

            def step(s, c, func, bias):
                act.wait_ge(act_mm, s + 1)
                nc.scalar.activation(g_f[:, c, :], act_ps[:, :], func, bias=bias).then_inc(g_ok, 1)
                act.wait_ge(h_ok, s + 1)
                if not isinstance(s, int) or s >= 2:
                    act.wait_ge(down_mm, s - 1)
                nc.scalar.activation(h_hi[:, c, :], h_f[:, c, :], ACT.Copy).then_inc(hhi_ok, 1)

            def l3_evac(b, j):
                half = 3 * P
                for n in range(2):
                    act.wait_ge(l3_tp, 2 * (b * L3U + j) + n + 1)
                    nc.scalar.activation(l3_w[:, b, j, n * half:(n + 1) * half], tp_ps[n][:, 0:half], ACT.Copy
                                         ).then_inc(l3_ok, 1)

            def x3_high(b, c):
                for m in range(KD):
                    act.wait_ge(acc_out, (b * CH + c) * KD + m + 1)
                    nc.scalar.activation(x_hi[:, m, tokens(b, c)], x_f[:, m, tokens(b, c)], ACT.Copy
                                         ).then_inc(x3_hi, 1)

            def l2_pass(p, begins=None, last=False, between=()):
                for j in range(UPP):
                    for c in range(CH):
                        step(p * UPP * CH + j * CH + c, c, ACT.Gelu_apprx_tanh, 0.0)
                        s = j * CH + c
                        if s < len(between):
                            between[s]()
                        if begins is not None and s < L3U:
                            l3_evac(begins, s)
                            if 1 <= s <= CH:
                                x3_high(begins, s - 1)
                        if c == 0:
                            if j + 1 < UPP:
                                l2_dn(p, j + 1)
                            elif last:
                                l3_dn(0, 0)
                            else:
                                l2_dn(p + 1, 0)
                        elif j + 2 < UPP:
                            l2_gu(p, j + 2)
                        elif last:
                            l3_gu(0, j + 2 - UPP)
                        else:
                            l2_gu(p + 1, j + 2 - UPP)

            l2_pass(0, between=start)
            with act.Fori(1, PASSES) as p:
                l2_pass(p)
            l2_pass(PASSES, begins=0)
            for p in range(PASSES + 1, 2 * PASSES):
                l2_pass(p, last=p == 2 * PASSES - 1)

            def out_copy(b, c, n=0):
                act.wait_ge(out_tp[n], b * CH + c + 1)
                t0 = c * TC + 2 * n
                nc.scalar.activation(x_nat[:, b, t0:t0 + 2, :].rearrange("p t d -> p (t d)"),
                                     tp_ps[n][:, :], ACT.Copy).then_inc(out_ok[n], 1)

            for b in range(B):
                act.wait_ge(s_bias[b], 48)
                for j in range(L3U):
                    for c in range(CH):
                        s = j * CH + c
                        step(CH * UNIT0[2 + b] + s, c, ACT.Silu, bu_col[:, b, j:j + 1])
                        if b == 0 and s < L3U:
                            l3_evac(1, s)
                            if 1 <= s <= CH:
                                x3_high(1, s - 1)
                        if b == 1 and 1 <= s <= CH:
                            out_copy(0, s - 1)
                        nb, nj = (b, j + 1 + c) if j + 1 + c < L3U else (b + 1, j + 1 + c - L3U)
                        if nb < B:
                            (l3_gu if c else l3_dn)(nb, nj)
            out_copy(1, 0)
            out_copy(1, 0, n=1)
            out_copy(1, 1)

        @block.tensor
        def _(pe):
            pe.wait_ge(ident_ok, 1)
            def w1_sum(g):
                pe.wait_ge(s_l1[g // 2], 16)
                pe.wait_ge(diag_ok, g + 1)
                for k in range(KD):
                    for o in range(KD):
                        mm = nc.tensor.matmul(tp_ps[k][:, o * P:(o + 1) * P], l1_nat[:, g, o, k * P:(k + 1) * P],
                                              diag[:, g, :], start=(g == 0 and o == 0), stop=(g == G - 1),
                                              skip_group_check=True)
                    if g == G - 1:
                        mm.then_inc(w1_mm, 1)

            for g in range(4):
                w1_sum(g)
            pe.wait_ge(s_bs, 32)
            for k in range(KD):
                mm = nc.tensor.transpose(banks[5][:, k * P:(k + 1) * P],
                                         bs_nat[:, k, :, :].rearrange("p e r -> p (e r)"), ident[:, :])
            mm.then_inc(bst_tp, 1)
            for g in range(4, 6):
                w1_sum(g)
            pe.wait_ge(s_mask, 16)
            for k in range(KD):
                for o in range(KD):
                    mm = nc.tensor.transpose(banks[4][:, k * D + o * P:k * D + (o + 1) * P],
                                             mask_nat[:, o, k * P:(k + 1) * P], ident[:, :])
            mm.then_inc(maskt_tp, 1)
            pe.wait_ge(bst_ok, 1)
            pe.wait_ge(asw_ok, B)
            for k in range(KD):
                nc.tensor.matmul(banks[2 * k + 1][:, :], bs_t[:, k * P:(k + 1) * P],
                                 as_w[:, :, :].rearrange("p b c -> p (b c)"), start=True, stop=True
                                 ).then_inc(w0_mm, 1)

            def xt(b, c):
                pe.wait_ge(s_x[b][c], 16)
                for k in range(KD):
                    for t in range(TC):
                        mm = nc.tensor.transpose(xt_bank(b, c, k)[:, t * P:(t + 1) * P],
                                                 x_nat[:, b, c * TC + t, k * P:(k + 1) * P], ident[:, :])
                    mm.then_inc(xt_tp, 1)

            def m_product(b):
                for cb in range(KD):
                    for k in range(KD):
                        mm = nc.tensor.matmul(m_bank(b)[:, cb * D:(cb + 1) * D],
                                              w0i[:, k, b, cb * P:(cb + 1) * P], w1it[:, k, b, :],
                                              start=(k == 0), stop=(k == KD - 1), skip_group_check=True)
                mm.then_inc(m_mm, 1)
                for m in range(KD):
                    for k in range(KD):
                        mm = nc.tensor.matmul(be_bank(b)[:, m:m + 1],
                                              w1it[:, k, b, m * P:(m + 1) * P], b0_col[:, k:k + 1],
                                              start=(k == 0), stop=(k == KD - 1), skip_group_check=True)
                mm.then_inc(be_mm, 1)

            def x2(b, c):
                pe.wait_ge(xt_lo, (b * CH + c + 1) * KD)
                pe.wait_ge(mhi_ok, b + 1)
                for m in range(KD):
                    n = 0
                    for w, y in ((m_hi, x_hi), (m_lo, x_hi), (m_hi, x_lo)):
                        if m == 0 and w is m_lo:
                            pe.wait_ge(mlo_ok, b + 1)
                        for k in range(KD):
                            mm = nc.tensor.matmul(x2_bank(b, c, m)[:, :], w[:, b, k, m * P:(m + 1) * P],
                                                  y[:, k, tokens(b, c)], start=(n == 0),
                                                  stop=(n == 3 * KD - 1))
                            n += 1
                    mm.then_inc(x2_mm, 1)

            xt(0, 0)
            pe.wait_ge(w1n_ok, KD)
            pe.wait_ge(maskt_ok, 1)
            for k in range(KD):
                for o in range(KD):
                    mm = nc.tensor.transpose(banks[4][:, k * D + o * P:k * D + (o + 1) * P],
                                             w1_nat[:, o, k * P:(k + 1) * P], ident[:, :])
            mm.then_inc(w1t_tp, 1)
            pe.wait_ge(w0_ok, KD * B)
            xt(0, 1)
            pe.wait_ge(s_b0, 16)
            pe.wait_ge(w1_ok, 1)
            m_product(0)
            for g in range(6, G):
                w1_sum(g)
            for c in range(CH):
                x2(0, c)

            def start_before(i):
                if i == 0:
                    pe.wait_ge(w1b_ok, KD)
                    m_product(1)
                elif i <= CH:
                    pe.wait_ge(mlo_ok, B)
                    pe.wait_ge(be_ok, B)
                    pe.wait_ge(xt_lo, (CH + i - 1) * KD)
                    xt(1, i - 1)
                else:
                    pe.wait_ge(xt_lo, 2 * CH * KD)
                    x2(1, 0)

            def start_after(i):
                if i == CH + 1:
                    pe.wait_ge(x2_f, (CH + 1) * KD)
                    x2(1, 1)

            def gate_up(s, slot, b, c, weights_lo=None, tokens_lo=None):
                for a, bank, free, made in ((0, act_ps, g_ok, act_mm), (1, lin_ps, h_ok, lin_mm)):
                    if not isinstance(s, int) or s >= 1:
                        pe.wait_ge(free, s)
                    n = 0
                    for w, y in ((gu_hi, x_hi), (gu_lo, x_hi), (gu_hi, x_lo)):
                        if a == 0 and w is gu_lo and weights_lo is not None:
                            pe.wait_ge(gulo_ok, weights_lo)
                        if a == 0 and y is x_lo and tokens_lo is not None:
                            pe.wait_ge(*tokens_lo)
                        for k in range(KD):
                            mm = nc.tensor.matmul(bank[:, :], w[:, slot, a * KD + k, :], y[:, k, tokens(b, c)],
                                                  start=(n == 0), stop=(n == 3 * KD - 1))
                            n += 1
                    mm.then_inc(made, 1)

            def down(s, u, slot, c, start, stop):
                pe.wait_ge(dnlo_ok, u + 1)
                pe.wait_ge(hhi_ok, s + 1)
                for m in range(KD):
                    for w in (dn_lo, dn_hi):
                        nc.tensor.matmul(acc[2 * m + c][:, :], w[:, slot, m * P:(m + 1) * P], h_hi[:, c, :],
                                         start=start and w is dn_lo, stop=False, skip_group_check=True)
                pe.wait_ge(hlo_ok, s + 1)
                for m in range(KD):
                    mm = nc.tensor.matmul(acc[2 * m + c][:, :], dn_hi[:, slot, m * P:(m + 1) * P], h_lo[:, c, :],
                                          start=False, stop=stop, skip_group_check=True)
                mm.then_inc(down_mm, 1)

            def two_units(u, b, group=None, last=False, hook=None, before=None):
                for i in range(2 * CH):
                    s = u * CH + i
                    weights_lo = tokens_lo = None
                    if i % CH == 0:
                        pe.wait_ge(guhi_ok, u + i // CH + 1)
                        weights_lo = u + i // CH + 1
                    if group is not None and i < CH:
                        hi_ok, lo_ok = (x2_hi, x2_lo) if group < B else (x3_hi, x3_lo)
                        pe.wait_ge(hi_ok, KD * (CH * b + i + 1))
                        tokens_lo = lo_ok, KD * (CH * b + i + 1)
                    gate_up(s, i // CH, b, i % CH, weights_lo, tokens_lo)
                    if before:
                        before(i)
                    if not (group == 0 and i == 0):
                        if group is not None and group > 0 and 1 <= i <= CH:
                            pe.wait_ge(acc_out, KD * (CH * (group - 1) + i))
                        if group == 0 and i == 1:
                            pe.wait_ge(x2_f, KD * CH)
                        down_slot = ((i - 1) // CH) % 2
                        down(s - 1, u + (i - 1) // CH, down_slot, (i - 1) % CH,
                             group is not None and 1 <= i <= CH,
                             (group is not None and group > 0 and i == 0) or (last and i == 2 * CH - 1))
                    if hook:
                        hook(i)

            def l3_transposes(b, j):
                if j == 0:
                    pe.wait_ge(s_l3[b], 48)
                blocks = [l3_ug[:, b, a, j, k * P:(k + 1) * P] for a in range(2) for k in range(KD)]
                blocks += [l3_dn[:, b, m, j * P:(j + 1) * P] for m in range(KD)]
                for n in range(2):
                    if b or j:
                        pe.wait_ge(l3_ok, 2 * (b * L3U + j) + n - 1)
                    for i in range(3):
                        mm = nc.tensor.transpose(tp_ps[n][:, i * P:(i + 1) * P], blocks[3 * n + i], ident[:, :])
                    mm.then_inc(l3_tp, 1)

            def out_transposes(b, c):
                pe.wait_ge(acc_out, KD * (CH * (B + b) + c + 1))
                for n in range(2):
                    if b * CH + c:
                        pe.wait_ge(out_ok[n], b * CH + c)
                    else:
                        pe.wait_ge(l3_ok, 2 * B * L3U)
                    for i in range(2):
                        t0 = b * T + (c * TC + 2 * n + i) * P
                        for m in range(KD):
                            mm = nc.tensor.transpose(tp_ps[n][:, i * D + m * P:i * D + (m + 1) * P],
                                                     x_f[:, m, t0:t0 + P], ident[:, :])
                    mm.then_inc(out_tp[n], 1)

            for b in range(B):
                u0 = UNIT0[b]
                two_units(u0, b, group=b, before=None if b else start_before,
                          hook=(lambda i: l3_transposes(0, i)) if b else start_after)
                with pe.Fori(u0 + 2, u0 + G2U, 2) as u:
                    two_units(u, b)
            for b in range(B):
                u0 = UNIT0[B + b]
                two_units(u0, b, group=B + b,
                          hook=(lambda i: l3_transposes(1, i)) if b == 0 else
                          (lambda i: out_transposes(0, i - 1) if 1 <= i <= CH else None))
                two_units(u0 + 2, b, last=True)
            down(END[3] - 1, UNIT0[4] - 1, 1, CH - 1, False, True)
            out_transposes(1, 0)
            out_transposes(1, 1)

        @block.vector
        def _(dve):
            dve.wait_ge(s_cond, 16)
            for b in range(B):
                nc.vector.max(top_v[:, b, :], cond_r[:, b, :]).then_inc(r_max, 1)
            for b in range(B):
                dve.wait_ge(r_max, b + 1)
                nc.vector.max_index(top_i[:, b, :], top_v[:, b, :], cond_r[:, b, :]).then_inc(r_idx, 1)
                nc.vector.tensor_scalar(neg_m[:, b:b + 1], top_v[:, b, 0:1], -1.0, None, ALU.mult).then_inc(r_neg, 1)
            for g in range(G):
                dve.wait_ge(s_l1[g // 2], 16)
                if g == 0:
                    nc.vector.tensor_scalar(w1_nat[:, :, :], l1_nat[:, 0, :, :], cond_r[:, 0, 0:1], None, ALU.mult
                                            ).then_inc(w1n_sum, 1)
                else:
                    dve.wait_ge(w1n_sum, g)
                    nc.vector.scalar_tensor_tensor(out=w1_nat[:, :, :], in0=l1_nat[:, g, :, :],
                                                   scalar=cond_r[:, 0, g:g + 1], in1=w1_nat[:, :, :],
                                                   op0=ALU.mult, op1=ALU.add).then_inc(w1n_sum, 1)
            dve.wait_ge(s_mask, 16)
            dve.wait_ge(w1n_sum, G)
            nc.vector.tensor_tensor(w1_nat[:, :, :], w1_nat[:, :, :], mask_nat[:, :, :], ALU.mult
                                    ).then_inc(w1n_masked, 1)
            dve.wait_ge(s_wb, 16)
            dve.wait_ge(ident_ok, 1)
            for k in range(KD):
                nc.vector.tensor_tensor(wb[:, k, k * P:(k + 1) * P], wb[:, k, k * P:(k + 1) * P], ident[:, :],
                                        ALU.add).then_inc(wbi_ok, 1)
            dve.wait_ge(w1n_masked, 1)
            for k in range(KD):
                nc.vector.tensor_tensor(w1_nat[:, k, k * P:(k + 1) * P], w1_nat[:, k, k * P:(k + 1) * P],
                                        ident[:, :], ALU.add).then_inc(w1n_ok, 1)
            dve.wait_ge(wbi_ok, KD)
            for k in range(KD):
                dve.wait_ge(w0_mm, k + 1)
                for b in range(B):
                    nc.vector.tensor_tensor(w0i[:, k, b, :], banks[2 * k + 1][:, b * D:(b + 1) * D], wb[:, k, :],
                                            ALU.add).then_inc(w0_ok, 1)

            dve.wait_ge(r_exp, B)
            nc.vector.reciprocal(r_inv[:, :], r_sum[:, :]).then_inc(r_inv_ok, 1)
            dve.wait_ge(r_inv_ok, 1)
            for b in range(B):
                nc.vector.tensor_scalar(top_p[:, b, :], top_e[:, b, 0:2], r_inv[:, b:b + 1], None, ALU.mult
                                        ).then_inc(r_p, 1)
            dve.wait_ge(r_p, B)
            nc.vector.tensor_tensor(r_sum[:, :], top_p[:, :, 0], top_p[:, :, 1], ALU.add).then_inc(r_s2, 1)
            dve.wait_ge(r_s2, 1)
            nc.vector.reciprocal(r_inv[:, :], r_sum[:, :]).then_inc(r_inv_ok, 1)
            dve.wait_ge(r_inv_ok, 2)
            nc.vector.memset(w_pass[:, :, 0:1], 1.0).then_inc(r_w, 1)
            for b in range(B):
                nc.vector.tensor_scalar(w_raw[:, b, :], top_p[:, b, :], r_inv[:, b:b + 1], None, ALU.mult
                                        ).then_inc(r_w, 1)
            dve.wait_ge(r_w, 1 + B)
            nc.vector.tensor_scalar(w_part[:, :, :], w_raw[:, :, :], 1.0 - MOE_SCALE, None, ALU.mult).then_inc(r_w, 1)
            dve.wait_ge(r_w, 2 + B)
            nc.vector.scalar_tensor_tensor(out=w_pass[:, :, 1:PASSES], in0=w_raw[:, :, :], scalar=MOE_SCALE,
                                           in1=w_part[:, :, :], op0=ALU.mult, op1=ALU.add).then_inc(r_w, 1)

            def xt_low(b, c):
                for k in range(KD):
                    dve.wait_ge(xt_hi, (b * CH + c) * KD + k + 1)
                    nc.vector.tensor_tensor(x_lo[:, k, tokens(b, c)], xt_bank(b, c, k)[:, :],
                                            x_hi[:, k, tokens(b, c)].bitcast(F32), ALU.subtract).then_inc(xt_lo, 1)

            def m_low(b):
                dve.wait_ge(mhi_ok, b + 1)
                nc.vector.tensor_tensor(m_lo[:, b, :, :].rearrange("p k d -> p (k d)"), m_bank(b)[:, :],
                                        m_hi[:, b, :, :].rearrange("p k d -> p (k d)").bitcast(F32),
                                        ALU.subtract).then_inc(mlo_ok, 1)
                dve.wait_ge(be_mm, b + 1)
                dve.wait_ge(s_b1, 16)
                nc.vector.tensor_tensor(b_eff[:, b, :], be_bank(b)[:, 0:KD], b1_col[:, :], ALU.add).then_inc(be_ok, 1)

            def x2_low(b, c):
                dve.wait_ge(x2_mm, (b * CH + c + 1) * KD)
                dve.wait_ge(be_ok, b + 1)
                for m in range(KD):
                    nc.vector.tensor_scalar(x_f[:, m, tokens(b, c)], x2_bank(b, c, m)[:, :],
                                            b_eff[:, b, m:m + 1], None, ALU.add).then_inc(x2_f, 1)
                for m in range(KD):
                    dve.wait_ge(x2_hi, (b * CH + c) * KD + m + 1)
                    nc.vector.tensor_tensor(x_lo[:, m, tokens(b, c)], x_f[:, m, tokens(b, c)],
                                            x_hi[:, m, tokens(b, c)].bitcast(F32), ALU.subtract).then_inc(x2_lo, 1)

            xt_low(0, 0)
            xt_low(0, 1)

            m_low(0)
            dve.wait_ge(maskt_ok, 1)
            for k in range(KD):
                dve.wait_ge(w1_mm, k + 1)
                nc.vector.tensor_tensor(w1it[:, k, 1, :], tp_ps[k][:, 0:D], mask_t[:, k, :], ALU.mult
                                        ).then_inc(w1_masked, 1)
            for k in range(KD):
                dve.wait_ge(w1_masked, k + 1)
                nc.vector.tensor_tensor(w1it[:, k, 1, k * P:(k + 1) * P], w1it[:, k, 1, k * P:(k + 1) * P],
                                        ident[:, :], ALU.add).then_inc(w1b_ok, 1)
            x2_low(0, 0)
            x2_low(0, 1)

            def step(s, c, layer, w, between=None):
                dve.wait_ge(lin_mm, s + 1)
                dve.wait_ge(g_ok, s + 1)
                if layer == 2:
                    nc.vector.scalar_tensor_tensor(out=h_f[:, c, :], in0=g_f[:, c, :], scalar=w, in1=lin_ps[:, :],
                                                   op0=ALU.mult, op1=ALU.mult).then_inc(h_ok, 1)
                else:
                    nc.vector.scalar_tensor_tensor(out=h_f[:, c, :], in0=lin_ps[:, :], scalar=w, in1=g_f[:, c, :],
                                                   op0=ALU.add, op1=ALU.mult).then_inc(h_ok, 1)
                if between:
                    between()
                dve.wait_ge(hhi_ok, s + 1)
                nc.vector.tensor_tensor(h_lo[:, c, :], h_f[:, c, :], h_hi[:, c, :].bitcast(F32), ALU.subtract
                                        ).then_inc(hlo_ok, 1)

            def take(group, b, c, blocks=range(KD)):
                dve.wait_ge(down_mm, END[group] - 1 + c)
                for m in blocks:
                    if group < B:
                        nc.vector.tensor_tensor(x_f[:, m, tokens(b, c)], acc[2 * m + c][:, :],
                                                x_f[:, m, tokens(b, c)], ALU.add).then_inc(acc_out, 1)
                    else:
                        nc.vector.scalar_tensor_tensor(out=x_f[:, m, tokens(b, c)], in0=acc[2 * m + c][:, :],
                                                       scalar=bd_col[:, b, m:m + 1], in1=x_f[:, m, tokens(b, c)],
                                                       op0=ALU.add, op1=ALU.add).then_inc(acc_out, 1)

            def out_copy(b, c):
                dve.wait_ge(out_tp[1], b * CH + c + 1)
                nc.vector.tensor_copy(x_nat[:, b, c * TC + 2:c * TC + 4, :].rearrange("p t d -> p (t d)"),
                                      tp_ps[1][:, :]).then_inc(out_ok[1], 1)

            def l2_units(b, p, first):
                with dve.Fori(first, UPP) as j:
                    for c in range(CH):
                        step((b * PASSES + p) * UPP * CH + j * CH + c, c, 2, w_pass[:, b, bass.ds(p, 1)])

            dve.wait_ge(r_w, 3 + B)
            start = [lambda: m_low(1), lambda: xt_low(1, 0), lambda: xt_low(1, 1),
                     lambda: x2_low(1, 0), lambda: x2_low(1, 1)]
            for s in range(3 * CH):
                step(s, s % CH, 2, w_pass[:, 0, 0:1])
                if s < len(start):
                    start[s]()
            l2_units(0, 0, 3)
            with dve.Fori(1, PASSES) as p:
                l2_units(0, p, 0)
            for c in range(CH):
                take(0, 0, c)
                step(END[0] + c, c, 2, w_pass[:, 1, 0:1])
            l2_units(1, 0, 1)
            with dve.Fori(1, PASSES) as p:
                l2_units(1, p, 0)
            for b in range(B):
                dve.wait_ge(s_bias[b], 48)
                for j in range(L3U):
                    for c in range(CH):
                        if j == 0:
                            take(1 + b, 1 - b, c)
                        s = CH * UNIT0[2 + b] + j * CH + c
                        step(s, c, 3, bg_col[:, b, j:j + 1],
                             (lambda: take(3, 1, 0, [0])) if s == END[3] - 1 else None)
                        if b == 1 and 1 <= j * CH + c <= CH:
                            out_copy(0, j * CH + c - 1)
            take(3, 1, 0, [1])
            take(3, 1, 1)
            out_copy(1, 1)


_INS = ['x', 'cond_8', 'L0_cond_W_base', 'L0_cond_b_base', 'L0_cond_As', 'L0_cond_Bs', 'L1_cond_weight',
        'L1_cond_mask', 'L1_cond_bias', 'L2_cond_skill_gate', 'L2_cond_skill_up', 'L2_cond_skill_down',
        'L2_cond_shared_gate', 'L2_cond_shared_up', 'L2_cond_shared_down', 'L3_cond_W_up', 'L3_cond_b_up',
        'L3_cond_W_gate', 'L3_cond_b_gate', 'L3_cond_W_down', 'L3_cond_b_down']


def kernel(**inputs):
    import numpy as _np
    import concourse.bacc as _bacc
    from concourse import mybir as _mybir
    from concourse.bass_utils import run_bass_kernel_spmd as _run

    nc = _bacc.Bacc("TRN2", target_bir_lowering=False, num_devices=1)
    arrays, args = {}, []
    for name in _INS:
        a = _np.ascontiguousarray(inputs[name])
        arrays[f"in_{name}_dram"] = a
        args.append(nc.dram_tensor(f"in_{name}_dram", a.shape, _mybir.dt.from_np(a.dtype), kind="ExternalInput").ap())
    x = inputs['x']
    args.append(nc.dram_tensor("out_dram", x.shape, _mybir.dt.from_np(_np.dtype(x.dtype)), kind="ExternalOutput").ap())
    cond_residual_stack(nc, *args)
    r = _run(nc, [arrays], core_ids=[0])
    return r.results[0]["out_dram"]
```
